# Optimizing a Trainium2 kernel written in Bass

```python
import numpy as np
import jax
import jax.numpy as jnp

def _softmax(x, axis=-1):
    return jax.nn.softmax(x, axis=axis)

def _gelu(x):
    return jax.nn.gelu(x, approximate=True)

def _silu(x):
    return jax.nn.silu(x)

def _sigmoid(x):
    return jax.nn.sigmoid(x)

def _layernorm(x, axis=-1, eps=1e-05):
    m = jnp.mean(x, axis=axis, keepdims=True)
    v = jnp.var(x, axis=axis, keepdims=True)
    return (x - m) / jnp.sqrt(v + eps)

def _scatter_add(tgt, idx, src, axis=0):
    return tgt.at[idx].add(src)

def _segment_sum(src, seg, n):
    return jax.ops.segment_sum(src, seg, n)
kernel_name = 'mk_adaln_ffn_d1_seqx_r4_6d2b28'

def setup_inputs(seed: int=0):
    np.random.seed(seed)
    _w = jnp.asarray

    def _rec_inputs():
        import jax
        import jax.numpy as jnp
        _rk = jax.random.key(seed)
        x = -0.000125 + 0.9999 * jax.random.normal(jax.random.fold_in(_rk, 1), (8, 256, 1024), jnp.float32)
        _lenS = 256 - jax.random.randint(jax.random.fold_in(_rk, 7), (8,), 0, max(1, 256 // 4) + 1, jnp.int32)
        _lenS2 = 256 - jax.random.randint(jax.random.fold_in(_rk, 8), (8,), 0, max(1, 256 // 4) + 1, jnp.int32)
        itok_B_3_7 = jax.random.randint(jax.random.fold_in(_rk, 11), (8,), 3, 8, jnp.int32)
        return (x, itok_B_3_7)
    x, itok_B_3_7 = _rec_inputs()

    def _L0_cond_setup():
        import jax, jax.numpy as jnp
        import numpy as np
        RANK = 16
        ALPHA = 16.0
        SCALING = ALPHA / RANK
        N_ADAPTERS = 8
        IN_F = 1024
        OUT_F = 1024
        BATCH = 4
        SEQ = 512
        key = jax.random.key(seed)
        kx, ka, kb, ki = jax.random.split(key, 4)
        x = jax.random.normal(kx, (BATCH, SEQ, IN_F), dtype=jnp.float32)
        A = jax.random.normal(ka, (N_ADAPTERS, OUT_F, RANK), dtype=jnp.float32) * 0.02
        B = jax.random.normal(kb, (N_ADAPTERS, RANK, IN_F), dtype=jnp.float32) * 0.02
        adapter_ids = jax.random.randint(ki, (BATCH,), 0, N_ADAPTERS, dtype=jnp.int32)
        return {'x': x, 'A': A, 'B': B, 'adapter_ids': adapter_ids}
    _L0_cond_all = _L0_cond_setup()
    _L0_cond_in = {k: v for k, v in _L0_cond_all.items() if k in ('A', 'B')}
    del _L0_cond_all

    def _L0_ffn_setup():
        import jax, jax.numpy as jnp
        import numpy as np
        NUM_EXPERTS = 4
        HIDDEN = 1024
        RANK = 8
        ALPHA = 8.0
        SCALE = ALPHA / RANK
        key = jax.random.key(seed)
        ks = jax.random.split(key, 6)
        B, T, H, E, R = (4, 1024, HIDDEN, NUM_EXPERTS, RANK)
        x = jax.random.normal(ks[0], (B, T, H), dtype=jnp.float32)
        W_up = jax.random.normal(ks[1], (H, H), dtype=jnp.float32) / np.sqrt(H)
        gate_w = jax.random.normal(ks[2], (E, H), dtype=jnp.float32) / np.sqrt(H)
        expert_bias = jnp.zeros((E,), dtype=jnp.float32)
        lora_A = jax.random.normal(ks[3], (E, R, H), dtype=jnp.float32) / np.sqrt(H)
        lora_B = jax.random.normal(ks[4], (E, H, R), dtype=jnp.float32) * 0.01
        return {'x': x, 'W_up': W_up, 'gate_w': gate_w, 'expert_bias': expert_bias, 'lora_A': lora_A, 'lora_B': lora_B}
    _L0_ffn_all = _L0_ffn_setup()
    _L0_ffn_in = {k: v for k, v in _L0_ffn_all.items() if k in ('W_up', 'gate_w', 'expert_bias', 'lora_A', 'lora_B')}
    del _L0_ffn_all
    return {'x': x, 'itok_B_3_7': itok_B_3_7, 'L0_cond_A': _L0_cond_in['A'], 'L0_cond_B': _L0_cond_in['B'], 'L0_ffn_W_up': _L0_ffn_in['W_up'], 'L0_ffn_gate_w': _L0_ffn_in['gate_w'], 'L0_ffn_expert_bias': _L0_ffn_in['expert_bias'], 'L0_ffn_lora_A': _L0_ffn_in['lora_A'], 'L0_ffn_lora_B': _L0_ffn_in['lora_B']}

def reference(x, itok_B_3_7, L0_cond_A, L0_cond_B, L0_ffn_W_up, L0_ffn_gate_w, L0_ffn_expert_bias, L0_ffn_lora_A, L0_ffn_lora_B):
    import jax
    import jax.numpy as jnp

    def _L0_cond_ref(x, A, B, adapter_ids):
        import jax, jax.numpy as jnp
        import numpy as np
        RANK = 16
        ALPHA = 16.0
        SCALING = ALPHA / RANK
        N_ADAPTERS = 8
        IN_F = 1024
        OUT_F = 1024
        BATCH = 4
        SEQ = 512
        B_sel = B[adapter_ids]
        A_sel = A[adapter_ids]
        Bx = jnp.einsum('bni,bri->bnr', x, B_sel)
        out = jnp.einsum('bnr,bor->bno', Bx, A_sel)
        return out * SCALING

    def _L0_ffn_ref(x, W_up, gate_w, expert_bias, lora_A, lora_B):
        import jax, jax.numpy as jnp
        import numpy as np
        NUM_EXPERTS = 4
        HIDDEN = 1024
        RANK = 8
        ALPHA = 8.0
        SCALE = ALPHA / RANK
        B, T, H = x.shape
        E = gate_w.shape[0]
        x_flat = x.reshape(-1, H)
        logits = x_flat @ gate_w.T + expert_bias
        top1 = jnp.argmax(logits, axis=-1)
        one_hot = jax.nn.one_hot(top1, E, dtype=x_flat.dtype)
        base_out = jnp.einsum('bth,oh->bto', x, W_up)
        z = jnp.einsum('nh,erh->ner', x_flat, lora_A)
        d = jnp.einsum('ner,ehr->neh', z, lora_B) * SCALE
        delta = jnp.einsum('neh,ne->nh', d, one_hot)
        return base_out + delta.reshape(B, T, H)
    x = x + _L0_ffn_ref(_L0_cond_ref(x, L0_cond_A, L0_cond_B, itok_B_3_7), L0_ffn_W_up, L0_ffn_gate_w, L0_ffn_expert_bias, L0_ffn_lora_A, L0_ffn_lora_B)
    return x

_drawn_inputs = setup_inputs


def setup_inputs(seed=0):
    import zlib

    import numpy as np

    out = dict(_drawn_inputs(seed))
    spreads = {'L0_ffn_expert_bias': (0.0, 0.8)}
    factors = {'L0_ffn_gate_w': 8.0, 'L0_ffn_lora_A': 8.0, 'L0_ffn_lora_B': 8.0}
    for name, (base, spread) in spreads.items():
        noise = np.random.default_rng([zlib.crc32(name.encode()), seed]).standard_normal(out[name].shape)
        drawn = base * np.exp(spread * noise) if base else spread * noise
        out[name] = jnp.asarray(drawn.astype(out[name].dtype))
    for name, factor in factors.items():
        out[name] = (out[name] * factor).astype(out[name].dtype)
    return out
```

```python
from contextlib import ExitStack

import concourse.bass as bass
from concourse import mybir

F32 = mybir.dt.float32
BF16 = mybir.dt.bfloat16
ALU = mybir.AluOpType
P = 128
Q = 32
BANK = 512


def adaln_ffn(nc, x, ids, cond_a, cond_b, w_up, lora_a_gate, lora_b, bias_pairs, pair_votes,
              votes_needed, out):
    NB, _, KB, T = x.shape
    NA, _, _, R = cond_a.shape
    H = w_up.shape[3]
    ER = lora_b.shape[0]
    E = lora_a_gate.shape[2] - ER
    NPAIR = E * (E - 1) // 2
    G = ER + NPAIR
    NP2 = NB // 2
    WCH = w_up.shape[0]
    WK = KB // WCH
    HALF = H // 2
    assert 2 * R == Q and ER == Q and 4 * Q == P and KB == 8 and NB * R == P and HALF == BANK
    assert 2 * T == BANK

    with ExitStack() as ctx:
        def sb(name, shape, dt=F32):
            return ctx.enter_context(nc.sbuf_tensor(name, shape, dt))

        def sem(name):
            return ctx.enter_context(nc.semaphore(name))

        x_sb = sb("x_sb", [P, NB, KB * T])
        w_sb = sb("w_sb", [P, WCH, WK, H])
        a_raw = sb("a_raw", [P, NB, KB, R])
        a_sel = sb("a_sel", [P, KB, NB, R])
        b_sel = sb("b_sel", [P, NB, KB, R])
        b_pad = sb("b_pad", [P, NB, KB, Q])
        lg_sb = sb("lg_sb", [P, KB, ER + E])
        spread = sb("spread", [P, NP2, P // Q, Q])
        g_sb = sb("g_sb", [P, ER + E])
        g_rows = sb("g_rows", [P, G])
        u_map = sb("u_map", [P, NP2, Q + G])
        p_map = sb("p_map", [P, NP2, BANK])
        bias_sb = sb("bias_sb", [P, 2])
        margin = sb("margin", [P, 1])
        votes32 = sb("votes32", [P, P])
        votes = sb("votes", [P, P], BF16)
        needed = sb("needed", [P, 1])
        u_part = sb("u_part", [P, 2, T])
        uz = sb("uz", [P, 2, T])
        wins = sb("wins", [P, 2, T], BF16)
        v = sb("v", [P, 2, T])

        y_ps = ctx.enter_context(nc.psum_tensor("y_ps", [P, 2, 2, BANK], F32))
        part_ps = ctx.enter_context(nc.psum_tensor("part_ps", [P, BANK], F32))
        uzd_ps = ctx.enter_context(nc.psum_tensor("uzd_ps", [P, BANK], F32))
        count_ps = ctx.enter_context(nc.psum_tensor("count_ps", [P, BANK], F32))
        setup_ps = ctx.enter_context(nc.psum_tensor("setup_ps", [P, BANK], F32))

        x_loaded = [sem(f"x_loaded{b}") for b in range(NB)]
        w_loaded = [sem(f"w_loaded{c}") for c in range(WCH)]
        a_loaded = sem("a_loaded")
        b_loaded = sem("b_loaded")
        lg_loaded = sem("lg_loaded")
        lora_b_loaded = sem("lora_b_loaded")
        small_loaded = sem("small_loaded")
        stored = sem("stored")

        cleared = sem("cleared")
        eye_ready = sem("eye_ready")
        a_ready = sem("a_ready")
        b_padded = sem("b_padded")
        margin_ready = sem("margin_ready")
        votes_ready = sem("votes_ready")
        g_done = sem("g_done")
        g_copied = sem("g_copied")
        g_rows_ready = sem("g_rows_ready")
        u_map_done = sem("u_map_done")
        u_map_ready = sem("u_map_ready")
        lora_spread = sem("lora_spread")
        p_done = sem("p_done")
        p_low_ready = sem("p_low_ready")
        p_high_ready = sem("p_high_ready")

        parts_done = sem("parts_done")
        parts_copied = sem("parts_copied")
        uzd_done = sem("uzd_done")
        uz_copied = sem("uz_copied")
        wins_ready = sem("wins_ready")
        count_done = sem("count_done")
        v_ready = sem("v_ready")
        y_done = sem("y_done")
        y_added = sem("y_added")

        block = ctx.enter_context(nc.Block())

        @block.sync
        def _(sp):
            for c in range(WCH):
                sp.dma_start(w_sb[:, c], w_up[c]).then_inc(w_loaded[c], 16)
            for b in range(NB):
                sp.dma_start(x_sb[:, b], x[b]).then_inc(x_loaded[b], 16)
            for b in range(NB):
                sp.wait_ge(y_added, 2 * b + 2)
                sp.dma_start(out[b], x_sb[:, b]).then_inc(stored, 16)
            sp.wait_ge(stored, 16 * NB)

        @block.scalar
        def _(act):
            act.dma_start(lg_sb[:], lora_a_gate).then_inc(lg_loaded, 16)
            adapter = [act.value_load(ids[0:1, b:b + 1], min_val=0, max_val=NA - 1)
                       for b in range(NB)]
            for b in range(NB):
                act.dma_start(a_raw[:, b], cond_a[bass.ds(adapter[b], 1)]
                              .rearrange("a p k r -> (a p) k r")).then_inc(a_loaded, 16)
            for b in range(NB):
                act.dma_start(b_sel[:, b], cond_b[bass.ds(adapter[b], 1)]
                              .rearrange("a p k r -> (a p) k r")).then_inc(b_loaded, 16)
            act.dma_start(p_map[Q:2 * Q, 0], lora_b[:, 0:HALF]).then_inc(lora_b_loaded, 16)
            act.dma_start(p_map[3 * Q:P, 0], lora_b[:, HALF:H]).then_inc(lora_b_loaded, 16)
            act.dma_start(bias_sb[2 * Q:2 * Q + NPAIR], bias_pairs).then_inc(small_loaded, 16)
            act.dma_start(votes32[2 * Q:2 * Q + NPAIR], pair_votes).then_inc(small_loaded, 16)
            act.dma_start(needed[:], votes_needed).then_inc(small_loaded, 16)

            def copy_parts(b):
                act.wait_ge(parts_done, b + 1)
                if b >= 2:
                    act.wait_ge(uzd_done, b - 1)
                nc.scalar.copy(u_part[:, b % 2], part_ps[:, 0:T]).then_inc(parts_copied, 1)

            def copy_uz(b):
                act.wait_ge(uzd_done, b + 1)
                if b >= 2:
                    act.wait_ge(v_ready, b - 1)
                for half in range(2):
                    nc.scalar.copy(uz[2 * Q * half:2 * Q * (half + 1), b % 2],
                                   uzd_ps[0:2 * Q, 0:T]).then_inc(uz_copied, 1)

            act.wait_ge(lora_b_loaded, 32)
            for row in (Q, 3 * Q):
                nc.scalar.copy(p_map[row:row + Q, 1:NP2], p_map[row:row + Q, 0].unsqueeze(1)
                               .to_broadcast([Q, NP2 - 1, HALF])).then_inc(lora_spread, 1)

            act.wait_ge(p_done, 1)
            for j in range(NP2):
                nc.scalar.copy(p_map[0:Q, j], y_ps[Q * j:Q * (j + 1), 0, 0]).then_inc(p_low_ready, 1)
                if j == 0:
                    copy_parts(0)
                    copy_uz(0)
            for b in range(1, NB):
                copy_parts(b)
                copy_uz(b)

        @block.gpsimd
        def _(pool):
            nc.gpsimd.memset(b_pad[:], 0.0).then_inc(cleared, 1)
            nc.gpsimd.memset(spread[:], 0.0).then_inc(cleared, 1)
            nc.gpsimd.memset(u_map[:, :, 0:Q], 0.0).then_inc(cleared, 1)
            pool.wait_ge(cleared, 2)
            nc.gpsimd.affine_select(out=spread[:], in_=spread[:], compare_op=ALU.not_equal, fill=1.0,
                                    base=0, pattern=[[-Q, NP2], [0, P // Q], [-1, Q]],
                                    channel_multiplier=1).then_inc(eye_ready, 1)
            pool.wait_ge(cleared, 3)
            for c in range(P // Q):
                if c:
                    pool.wait_ge(eye_ready, 1 + c)
                nc.gpsimd.affine_select(out=u_map[:, :, 0:Q], in_=u_map[:, :, 0:Q],
                                        compare_op=ALU.not_equal, fill=1.0, base=-Q * c,
                                        pattern=[[0, NP2], [-1, Q]],
                                        channel_multiplier=1).then_inc(eye_ready, 1)

        @block.vector
        def _(dve):
            dve.wait_ge(a_loaded, 16 * NB)
            for half in range(2):
                ks = slice(KB // 2 * half, KB // 2 * (half + 1))
                nc.vector.tensor_copy(a_sel[:, ks].rearrange("p k b r -> p b k r"),
                                      a_raw[:, :, ks]).then_inc(a_ready, 1)
            dve.wait_ge(cleared, 1)
            dve.wait_ge(b_loaded, 16 * NB)
            for odd in range(2):
                nc.vector.tensor_copy(b_pad[:, odd::2, :, R * odd:R * (odd + 1)],
                                      b_sel[:, odd::2]).then_inc(b_padded, 1)
            rows = slice(2 * Q, 2 * Q + NPAIR)
            dve.wait_ge(small_loaded, 48)
            nc.vector.tensor_tensor(margin[rows], bias_sb[rows, 0:1], bias_sb[rows, 1:2],
                                    ALU.subtract).then_inc(margin_ready, 1)
            nc.vector.tensor_copy(votes[rows], votes32[rows]).then_inc(votes_ready, 1)
            dve.wait_ge(g_done, 1)
            nc.vector.tensor_copy(g_sb[:], setup_ps[:, 0:ER + E]).then_inc(g_copied, 1)
            dve.wait_ge(g_copied, 1)
            nc.vector.tensor_copy(g_rows[:, 0:ER], g_sb[:, 0:ER]).then_inc(g_rows_ready, 1)
            at = ER
            for e in range(E - 1):
                nc.vector.tensor_scalar(g_rows[:, at:at + E - 1 - e], g_sb[:, ER + e + 1:ER + E],
                                        g_sb[:, ER + e:ER + e + 1], None,
                                        ALU.subtract).then_inc(g_rows_ready, 1)
                at += E - 1 - e
            dve.wait_ge(u_map_done, 1)
            nc.vector.tensor_copy(u_map[:, :, Q:Q + G],
                                  setup_ps[:, 0:NP2 * G].rearrange("p (j g) -> p j g", j=NP2)
                                  ).then_inc(u_map_ready, 1)

            def find_wins(b):
                if b == 0:
                    dve.wait_ge(margin_ready, 1)
                dve.wait_ge(uzd_done, b + 1)
                if b >= 2:
                    dve.wait_ge(count_done, b - 1)
                nc.vector.tensor_scalar(wins[rows, b % 2], uzd_ps[rows, 0:T], margin[rows], None,
                                        ALU.is_le).then_inc(wins_ready, 1)

            def choose(b):
                dve.wait_ge(count_done, b + 1)
                dve.wait_ge(uz_copied, 2 * b + 2)
                if b >= 2:
                    dve.wait_ge(y_done, 2 * (b - 1))
                nc.vector.scalar_tensor_tensor(out=v[:, b % 2], in0=count_ps[:, 0:T],
                                               scalar=needed[:], in1=uz[:, b % 2],
                                               op0=ALU.is_ge, op1=ALU.mult).then_inc(v_ready, 1)

            def add_x(b, half):
                dve.wait_ge(y_done, 2 * b + half + 1)
                xs = x_sb[:, b].rearrange("p (h m n) -> p h m n", h=2, m=2)[:, :, half]
                nc.vector.tensor_tensor(xs, y_ps[:, half], xs, ALU.add).then_inc(y_added, 1)

            dve.wait_ge(p_done, 1)
            for j in range(NP2):
                nc.vector.tensor_copy(p_map[2 * Q:3 * Q, j],
                                      y_ps[Q * j:Q * (j + 1), 0, 1]).then_inc(p_high_ready, 1)
                if j == 0:
                    find_wins(0)
                    choose(0)
            for b in range(NB):
                add_x(b, 0)
                if b + 1 < NB:
                    find_wins(b + 1)
                    choose(b + 1)
                add_x(b, 1)

        @block.tensor
        def _(pe):
            pe.wait_ge(lg_loaded, 16)
            for k in range(KB):
                pe.wait_ge(a_ready, 2 * k // KB + 1)
                mm = nc.tensor.matmul(setup_ps[:, 0:ER + E], a_sel[:, k], lg_sb[:, k],
                                      start=(k == 0), stop=(k == KB - 1))
            mm.then_inc(g_done, 1)

            def multiply_w(c):
                pe.wait_ge(w_loaded[c], 16)
                for k in range(WK * c, WK * (c + 1)):
                    for half in range(2):
                        mm = nc.tensor.matmul(y_ps[:, 0, half], a_sel[:, k],
                                              w_sb[:, c, k % WK, HALF * half:HALF * (half + 1)],
                                              start=(k == 0), stop=(k == KB - 1))
                if c == WCH - 1:
                    mm.then_inc(p_done, 1)

            def spread_g():
                pe.wait_ge(g_rows_ready, E)
                pe.wait_ge(eye_ready, 1)
                for j in range(NP2):
                    mm = nc.tensor.matmul(setup_ps[:, G * j:G * (j + 1)],
                                          spread[:, j], g_rows[:], start=True, stop=True)
                mm.then_inc(u_map_done, 1)

            def multiply_b(b):
                if b == 0:
                    pe.wait_ge(b_padded, 2)
                else:
                    pe.wait_ge(parts_copied, b)
                pe.wait_ge(x_loaded[b], 16)
                for k in range(KB):
                    c = k % 4
                    mm = nc.tensor.matmul(part_ps[Q * c:Q * (c + 1), 0:T], b_pad[:, b, k],
                                          x_sb[:, b, T * k:T * (k + 1)],
                                          start=(k < 4), stop=(k >= 4))
                mm.then_inc(parts_done, 1)

            def make_uzd(b):
                pe.wait_ge(parts_copied, b + 1)
                if b == 0:
                    pe.wait_ge(u_map_ready, 1)
                    pe.wait_ge(eye_ready, 1 + P // Q)
                else:
                    pe.wait_ge(uz_copied, 2 * b)
                    pe.wait_ge(wins_ready, b)
                nc.tensor.matmul(uzd_ps[0:Q + G, 0:T], u_map[:, b // 2], u_part[:, b % 2],
                                 start=True, stop=True).then_inc(uzd_done, 1)

            def count_votes(b):
                pe.wait_ge(wins_ready, b + 1)
                if b == 0:
                    pe.wait_ge(votes_ready, 1)
                else:
                    pe.wait_ge(v_ready, b)
                nc.tensor.matmul(count_ps[:, 0:T], votes[2 * Q:2 * Q + NPAIR],
                                 wins[2 * Q:2 * Q + NPAIR, b % 2],
                                 start=True, stop=True).then_inc(count_done, 1)

            def make_y(b, half):
                if half == 0:
                    pe.wait_ge(v_ready, b + 1)
                    pe.wait_ge(p_low_ready, b // 2 + 1)
                    pe.wait_ge(p_high_ready, b // 2 + 1)
                    if b == 0:
                        pe.wait_ge(lora_b_loaded, 32)
                        pe.wait_ge(p_low_ready, NP2)
                        pe.wait_ge(p_high_ready, NP2)
                    if b == 2:
                        pe.wait_ge(lora_spread, 2)
                if b:
                    pe.wait_ge(y_added, 2 * (b - 1) + half + 1)
                for m in range(2):
                    for side in range(2):
                        rows = slice(2 * Q * side, 2 * Q * (side + 1))
                        o = P * (2 * half + m)
                        mm = nc.tensor.matmul(y_ps[:, half, side, T * m:T * (m + 1)],
                                              p_map[rows, b // 2, o:o + P], v[rows, b % 2],
                                              start=True, stop=True)
                mm.then_inc(y_done, 1)

            for c in range(WCH):
                multiply_w(c)
                if c == 0:
                    spread_g()
            multiply_b(0)
            make_uzd(0)
            count_votes(0)
            for b in range(NB):
                if b + 1 < NB:
                    multiply_b(b + 1)
                make_y(b, 0)
                if b + 1 < NB:
                    make_uzd(b + 1)
                make_y(b, 1)
                if b + 1 < NB:
                    count_votes(b + 1)


def kernel(x, itok_B_3_7, L0_cond_A, L0_cond_B, L0_ffn_W_up, L0_ffn_gate_w, L0_ffn_expert_bias,
           L0_ffn_lora_A, L0_ffn_lora_B):
    import numpy as np
    import concourse.bacc as bacc
    from concourse.bass_utils import run_bass_kernel_spmd

    x, ids = np.asarray(x), np.asarray(itok_B_3_7)
    A, B, W = np.asarray(L0_cond_A), np.asarray(L0_cond_B), np.asarray(L0_ffn_W_up)
    gate, bias = np.asarray(L0_ffn_gate_w), np.asarray(L0_ffn_expert_bias)
    lora_a, lora_b = np.asarray(L0_ffn_lora_A), np.asarray(L0_ffn_lora_B)
    NB, T, H = x.shape
    NA, _, R = A.shape
    E, RL, _ = lora_a.shape
    KB, WCH = H // P, 4

    first = [e for e in range(E) for f in range(e + 1, E)]
    second = [f for e in range(E) for f in range(e + 1, E)]
    votes = np.zeros((len(first), P), np.float32)
    needed = np.zeros((P, 1), np.float32)
    for side in (Q, 3 * Q):
        for e in range(E):
            cols = slice(side + RL * e, side + RL * (e + 1))
            needed[cols] = E - 1 - e
            for n, (a, b) in enumerate(zip(first, second)):
                votes[n, cols] = (a == e) * 1.0 - (b == e) * 1.0
    arrays = {
        "x": x.reshape(NB, T, KB, P).transpose(0, 3, 2, 1),
        "ids": ids.reshape(1, NB),
        "cond_a": A.reshape(NA, KB, P, R).transpose(0, 2, 1, 3),
        "cond_b": B.reshape(NA, R, KB, P).transpose(0, 3, 2, 1),
        "w_up": W.reshape(H, WCH, KB // WCH, P).transpose(1, 3, 2, 0),
        "lora_a_gate": np.concatenate([lora_a.reshape(E * RL, H), gate]).reshape(E * RL + E, KB, P)
        .transpose(2, 1, 0),
        "lora_b": lora_b.transpose(0, 2, 1).reshape(E * RL, H),
        "bias_pairs": np.stack([bias[first], bias[second]], axis=1),
        "pair_votes": votes,
        "votes_needed": needed,
    }
    nc = bacc.Bacc("TRN2", target_bir_lowering=False, num_devices=1)
    arrays = {f"in_{name}": np.ascontiguousarray(a) for name, a in arrays.items()}
    ins = [nc.dram_tensor(name, a.shape, mybir.dt.from_np(a.dtype), kind="ExternalInput").ap()
           for name, a in arrays.items()]
    y = nc.dram_tensor("out_y", (NB, P, KB, T), F32, kind="ExternalOutput").ap()
    adaln_ffn(nc, *ins, y)
    r = run_bass_kernel_spmd(nc, [arrays], core_ids=[0])
    return np.ascontiguousarray(r.results[0]["out_y"].transpose(0, 3, 2, 1)).reshape(NB, T, H)
```

```python
from contextlib import ExitStack

import concourse.bass as bass
from concourse import mybir

F32 = mybir.dt.float32
F32R = mybir.dt.float32r
BF16 = mybir.dt.bfloat16
ALU = mybir.AluOpType
P = 128
Q = 32
BANK = 512
WARM_UP = 12


def adaln_ffn(nc, x, ids, cond_a, cond_b, w_up, lora_a_gate, lora_b, bias_pairs, pair_votes,
              votes_needed, out):
    NP2, _, _, KH, T2 = x.shape
    NB, KB, T = 2 * NP2, 2 * KH, T2 // 2
    NA = cond_a.shape[1]
    R = cond_a.shape[2] // KB
    H = w_up.shape[3]
    ER = lora_b.shape[0]
    E = lora_a_gate.shape[2] - ER
    NPAIR = E * (E - 1) // 2
    G = ER + NPAIR
    NY = KB // 2
    WCH = w_up.shape[0]
    WK = KB // WCH
    HALF = H // 2
    assert 2 * R == Q and ER == Q and 4 * Q == P and KB == 8 and NB * R == P
    assert HALF == BANK and T2 == BANK

    with ExitStack() as ctx:
        def sb(name, shape, dt=F32):
            return ctx.enter_context(nc.sbuf_tensor(name, shape, dt))

        def sem(name):
            return ctx.enter_context(nc.semaphore(name))

        x_sb = sb("x_sb", [P, NP2, KB, T2])
        w_sb = sb("w_sb", [P, WCH, WK, H])
        a_all = sb("a_all", [P, NA, KB * R])
        b_all = sb("b_all", [P, NA, KB * R])
        a_sel = sb("a_sel", [P, KB, NB, R])
        b_pad = sb("b_pad", [P, NB, KB, Q])
        lg_sb = sb("lg_sb", [P, KB, ER + E])
        spread = sb("spread", [P, NP2, P // Q, Q])
        g_sb = sb("g_sb", [P, ER + E])
        g_rows = sb("g_rows", [P, G])
        u_map = sb("u_map", [P, NP2, Q + G])
        idle = sb("idle", [P, BANK], BF16)
        sums = sb("sums", [P, Q])
        lora_sb = sb("lora_sb", [P, H])
        p_map = sb("p_map", [P, NP2, H], F32R)
        bias_sb = sb("bias_sb", [P, 2])
        margin = sb("margin", [P, 1])
        votes32 = sb("votes32", [P, P])
        votes = sb("votes", [P, P], BF16)
        needed = sb("needed", [P, 1])
        u_part = sb("u_part", [P, 2, BANK])
        uz = sb("uz", [P, 2, BANK])
        wins = sb("wins", [P, 2, BANK], BF16)
        v_full = sb("v_full", [P, 2, BANK])
        v = sb("v", [P, 2, 2, BANK], F32R)

        y_ps = ctx.enter_context(nc.psum_tensor("y_ps", [P, 2, 2 * BANK], F32))
        p_ps = y_ps[:, 1]
        part_ps = ctx.enter_context(nc.psum_tensor("part_ps", [P, 2, BANK], F32))
        setup_ps = part_ps[:, 1]
        uzd_ps = ctx.enter_context(nc.psum_tensor("uzd_ps", [P, BANK], F32))
        count_ps = ctx.enter_context(nc.psum_tensor("count_ps", [P, BANK], F32))

        x_loaded = [sem(f"x_loaded{n}") for n in range(2 * NP2)]
        w_loaded = [sem(f"w_loaded{c}") for c in range(WCH)]
        a_loaded = sem("a_loaded")
        b_loaded = sem("b_loaded")
        lg_loaded = sem("lg_loaded")
        lora_b_loaded = sem("lora_b_loaded")
        small_loaded = sem("small_loaded")
        stored = sem("stored")

        cleared = sem("cleared")
        idle_ready = sem("idle_ready")
        eye_ready = sem("eye_ready")
        sums_ready = sem("sums_ready")
        a_ready = sem("a_ready")
        b_padded = sem("b_padded")
        margin_ready = sem("margin_ready")
        votes_ready = sem("votes_ready")
        g_done = sem("g_done")
        g_copied = sem("g_copied")
        g_rows_ready = sem("g_rows_ready")
        u_map_done = sem("u_map_done")
        u_map_ready = sem("u_map_ready")
        lora_high_ready = sem("lora_high_ready")
        lora_low_ready = sem("lora_low_ready")
        lora_spread = sem("lora_spread")
        p_done = sem("p_done")
        p_high_ready = sem("p_high_ready")
        p_low_ready = sem("p_low_ready")

        parts_done = sem("parts_done")
        parts_copied = sem("parts_copied")
        uzd_done = sem("uzd_done")
        uz_ready = sem("uz_ready")
        wins_ready = sem("wins_ready")
        count_done = sem("count_done")
        v_full_ready = sem("v_full_ready")
        v_high_ready = sem("v_high_ready")
        v_low_ready = sem("v_low_ready")
        y_done = sem("y_done")
        y_added = sem("y_added")

        block = ctx.enter_context(nc.Block())

        @block.sync
        def _(sp):
            sp.dma_start(a_all[:], cond_a).then_inc(a_loaded, 16)
            for c in range(WCH):
                sp.dma_start(w_sb[:, c], w_up[c]).then_inc(w_loaded[c], 16)
                if c == 0:
                    sp.dma_start(b_all[:], cond_b).then_inc(b_loaded, 16)
            for j in range(NP2):
                for half in range(2):
                    sp.dma_start(x_sb[:, j, KH * half:KH * (half + 1)],
                                 x[j, half]).then_inc(x_loaded[2 * j + half], 16)
            for j in range(NP2):
                for n in range(NY):
                    sp.wait_ge(y_added, NY * j + n + 1)
                    sp.dma_start(out[j, n], x_sb[:, j, 2 * n:2 * n + 2]).then_inc(stored, 16)
            sp.wait_ge(stored, 16 * NP2 * NY)

        @block.scalar
        def _(act):
            act.dma_start(lg_sb[:], lora_a_gate).then_inc(lg_loaded, 16)
            act.dma_start(lora_sb[Q:2 * Q], lora_b).then_inc(lora_b_loaded, 16)
            act.dma_start(bias_sb[2 * Q:2 * Q + NPAIR], bias_pairs).then_inc(small_loaded, 16)
            act.dma_start(votes32[2 * Q:2 * Q + NPAIR], pair_votes).then_inc(small_loaded, 16)
            act.dma_start(needed[:], votes_needed).then_inc(small_loaded, 16)

            def copy_parts(j):
                act.wait_ge(parts_done, 2 * (j + 1))
                if j >= 2:
                    act.wait_ge(uzd_done, j - 1)
                nc.scalar.copy(u_part[:, j % 2], part_ps[:, j % 2]).then_inc(parts_copied, 1)

            def copy_uz(j):
                act.wait_ge(uzd_done, j + 1)
                if j >= 2:
                    act.wait_ge(v_full_ready, j - 1)
                for at in (0, 2 * Q):
                    nc.scalar.copy(uz[at:at + 2 * Q, j % 2], uzd_ps[0:2 * Q]).then_inc(uz_ready, 1)

            def round_v(j):
                act.wait_ge(v_full_ready, j + 1)
                if j >= 2:
                    act.wait_ge(y_done, NY * (j - 1))
                nc.scalar.copy(v[:, j % 2, 0], v_full[:, j % 2]).then_inc(v_high_ready, 1)

            act.wait_ge(lora_b_loaded, 16)
            nc.scalar.copy(p_map[Q:2 * Q], lora_sb[Q:2 * Q].unsqueeze(1)
                           .to_broadcast([Q, NP2, H])).then_inc(lora_high_ready, 1)
            adapter = nc.values_load_multi_w_load_instructions(
                ids, [mybir.EngineType.Activation], min_val=0, max_val=NA - 1)[1]
            act.wait_ge(cleared, 1)
            act.wait_ge(b_loaded, 16)
            for b in range(NB):
                at = R * (b % 2)
                nc.scalar.copy(b_pad[:, b, :, at:at + R],
                               b_all[:, bass.ds(adapter[b], 1)]
                               .rearrange("p a (k r) -> p (a k) r", k=KB)).then_inc(b_padded, 1)
            act.wait_ge(lora_low_ready, 1)
            nc.scalar.copy(p_map[3 * Q:P, 1:NP2], p_map[3 * Q:P, 0].bitcast(F32).unsqueeze(1)
                           .to_broadcast([Q, NP2 - 1, H])).then_inc(lora_spread, 1)

            act.wait_ge(p_done, 1)
            for j in range(NP2):
                nc.scalar.copy(p_map[0:Q, j], p_ps[Q * j:Q * (j + 1)]).then_inc(p_high_ready, 1)
                if j == 1:
                    copy_parts(0)
                if j == 2:
                    copy_uz(0)
            round_v(0)
            copy_parts(1)
            for j in range(NP2 - 1):
                copy_uz(j + 1)
                round_v(j + 1)
                if j + 2 < NP2:
                    copy_parts(j + 2)

        @block.gpsimd
        def _(pool):
            nc.gpsimd.memset(b_pad[:], 0.0).then_inc(cleared, 1)
            nc.gpsimd.memset(spread[:], 0.0).then_inc(cleared, 1)
            nc.gpsimd.memset(sums[:], 0.0).then_inc(cleared, 1)
            pool.wait_ge(cleared, 2)
            nc.gpsimd.affine_select(out=spread[:], in_=spread[:], compare_op=ALU.not_equal, fill=1.0,
                                    base=0, pattern=[[-Q, NP2], [0, P // Q], [-1, Q]],
                                    channel_multiplier=1).then_inc(eye_ready, 1)
            pool.wait_ge(cleared, 3)
            for c in range(P // Q):
                if c:
                    pool.wait_ge(eye_ready, 1 + c)
                nc.gpsimd.affine_select(out=sums[:], in_=sums[:], compare_op=ALU.not_equal, fill=1.0,
                                        base=-Q * c, pattern=[[-1, Q]],
                                        channel_multiplier=1).then_inc(eye_ready, 1)
            pool.wait_ge(eye_ready, 1 + P // Q)
            nc.gpsimd.tensor_copy(u_map[:, :, 0:Q], sums[:].unsqueeze(1)
                                  .to_broadcast([P, NP2, Q])).then_inc(sums_ready, 1)

            pool.wait_ge(sums_ready, 1)
            for j in range(NP2):
                pool.wait_ge(v_high_ready, j + 1)
                if j:
                    pool.wait_ge(v_low_ready, j)
                if j >= 2:
                    pool.wait_ge(y_done, NY * (j - 1))
                nc.gpsimd.tensor_tensor(v[:, j % 2, 1], v_full[:, j % 2],
                                        v[:, j % 2, 0].bitcast(F32),
                                        ALU.subtract).then_inc(v_low_ready, 1)

        @block.vector
        def _(dve):
            nc.vector.memset(idle[:], 0.0).then_inc(idle_ready, 1)
            adapter = nc.values_load_multi_w_load_instructions(
                ids, [mybir.EngineType.DVE], min_val=0, max_val=NA - 1)[1]
            dve.wait_ge(a_loaded, 16)
            for b in range(NB):
                nc.vector.tensor_copy(a_sel[:, :, b],
                                      a_all[:, bass.ds(adapter[b], 1)]
                                      .rearrange("p a (k r) -> p (a k) r", k=KB)).then_inc(a_ready, 1)
            dve.wait_ge(g_done, 1)
            nc.vector.tensor_copy(g_sb[:], setup_ps[:, 0:ER + E]).then_inc(g_copied, 1)
            dve.wait_ge(g_copied, 1)
            nc.vector.tensor_copy(g_rows[:, 0:ER], g_sb[:, 0:ER]).then_inc(g_rows_ready, 1)
            at = ER
            for e in range(E - 1):
                nc.vector.tensor_scalar(g_rows[:, at:at + E - 1 - e], g_sb[:, ER + e + 1:ER + E],
                                        g_sb[:, ER + e:ER + e + 1], None,
                                        ALU.subtract).then_inc(g_rows_ready, 1)
                at += E - 1 - e
            dve.wait_ge(lora_b_loaded, 16)
            dve.wait_ge(lora_high_ready, 1)
            nc.vector.tensor_tensor(p_map[3 * Q:P, 0], lora_sb[Q:2 * Q],
                                    p_map[Q:2 * Q, 0].bitcast(F32),
                                    ALU.subtract).then_inc(lora_low_ready, 1)
            rows = slice(2 * Q, 2 * Q + NPAIR)
            dve.wait_ge(small_loaded, 48)
            nc.vector.tensor_tensor(margin[rows], bias_sb[rows, 0:1], bias_sb[rows, 1:2],
                                    ALU.subtract).then_inc(margin_ready, 1)
            nc.vector.tensor_copy(votes[rows], votes32[rows]).then_inc(votes_ready, 1)
            dve.wait_ge(u_map_done, 1)
            g_spread = setup_ps[:, 0:NP2 * G].rearrange("p (j g) -> p j g", j=NP2)
            nc.vector.tensor_copy(u_map[:, :, Q:Q + G], g_spread).then_inc(u_map_ready, 1)

            def find_wins(j):
                if j == 0:
                    dve.wait_ge(margin_ready, 1)
                dve.wait_ge(uzd_done, j + 1)
                if j >= 2:
                    dve.wait_ge(count_done, j - 1)
                nc.vector.tensor_scalar(wins[rows, j % 2], uzd_ps[rows], margin[rows], None,
                                        ALU.is_le).then_inc(wins_ready, 1)

            def choose(j):
                dve.wait_ge(count_done, j + 1)
                dve.wait_ge(uz_ready, 2 * j + 2)
                if j >= 2:
                    dve.wait_ge(v_low_ready, j - 1)
                nc.vector.scalar_tensor_tensor(out=v_full[:, j % 2], in0=count_ps[:],
                                               scalar=needed[:], in1=uz[:, j % 2],
                                               op0=ALU.is_ge, op1=ALU.mult).then_inc(v_full_ready, 1)

            def add_x(j, n):
                dve.wait_ge(y_done, NY * j + n + 1)
                xs = x_sb[:, j, 2 * n:2 * n + 2]
                ys = y_ps[:, n % 2].rearrange("p (o t) -> p o t", o=2)
                nc.vector.tensor_tensor(xs, ys, xs, ALU.add).then_inc(y_added, 1)

            dve.wait_ge(p_done, 1)
            for j in range(NP2):
                dve.wait_ge(p_high_ready, j + 1)
                nc.vector.tensor_tensor(p_map[2 * Q:3 * Q, j], p_ps[Q * j:Q * (j + 1)],
                                        p_map[0:Q, j].bitcast(F32),
                                        ALU.subtract).then_inc(p_low_ready, 1)
                if j == 1:
                    find_wins(0)
                if j == 2:
                    choose(0)
            for j in range(NP2):
                if j + 1 < NP2:
                    find_wins(j + 1)
                add_x(j, 0)
                if j + 1 < NP2:
                    choose(j + 1)
                for n in range(1, NY):
                    add_x(j, n)

        @block.tensor
        def _(pe):
            pe.wait_ge(idle_ready, 1)
            for _ in range(WARM_UP):
                nc.tensor.matmul(y_ps[:, 0, 0:BANK], idle[:, 0:P], idle[:], start=True, stop=True)
            pe.wait_ge(lg_loaded, 16)
            pe.wait_ge(a_ready, NB)
            for k in range(KB):
                mm = nc.tensor.matmul(setup_ps[:, 0:ER + E], a_sel[:, k], lg_sb[:, k],
                                      start=(k == 0), stop=(k == KB - 1))
            mm.then_inc(g_done, 1)

            def multiply_w(c):
                pe.wait_ge(w_loaded[c], 16)
                for k in range(WK * c, WK * (c + 1)):
                    for half in range(2):
                        mm = nc.tensor.matmul(p_ps[:, HALF * half:HALF * (half + 1)], a_sel[:, k],
                                              w_sb[:, c, k % WK, HALF * half:HALF * (half + 1)],
                                              start=(k == 0), stop=(k == KB - 1))
                if c == WCH - 1:
                    mm.then_inc(p_done, 1)

            def spread_g():
                pe.wait_ge(g_rows_ready, E)
                pe.wait_ge(eye_ready, 1)
                for j in range(NP2):
                    mm = nc.tensor.matmul(setup_ps[:, G * j:G * (j + 1)],
                                          spread[:, j], g_rows[:], start=True, stop=True)
                mm.then_inc(u_map_done, 1)

            def multiply_b(j, b):
                if b == 0:
                    if j == 0:
                        pe.wait_ge(b_padded, NB)
                    elif j >= 2:
                        pe.wait_ge(parts_copied, j - 1)
                    pe.wait_ge(x_loaded[2 * j], 16)
                    pe.wait_ge(x_loaded[2 * j + 1], 16)
                for k in range(KB):
                    c = k % 4
                    mm = nc.tensor.matmul(part_ps[Q * c:Q * (c + 1), j % 2, T * b:T * (b + 1)],
                                          b_pad[:, 2 * j + b, k],
                                          x_sb[:, j, k, T * b:T * (b + 1)],
                                          start=(k < 4), stop=(k >= 4))
                mm.then_inc(parts_done, 1)

            def make_uzd(j):
                pe.wait_ge(parts_copied, j + 1)
                if j == 0:
                    pe.wait_ge(u_map_ready, 1)
                    pe.wait_ge(sums_ready, 1)
                else:
                    pe.wait_ge(uz_ready, 2 * j)
                    pe.wait_ge(wins_ready, j)
                nc.tensor.matmul(uzd_ps[0:Q + G], u_map[:, j], u_part[:, j % 2],
                                 start=True, stop=True).then_inc(uzd_done, 1)

            rows = slice(2 * Q, 2 * Q + NPAIR)

            def count_votes(j):
                pe.wait_ge(wins_ready, j + 1)
                if j == 0:
                    pe.wait_ge(votes_ready, 1)
                else:
                    pe.wait_ge(v_full_ready, j)
                nc.tensor.matmul(count_ps[:], votes[rows], wins[rows, j % 2],
                                 start=True, stop=True).then_inc(count_done, 1)

            def make_y(j, n):
                if n == 0:
                    pe.wait_ge(v_low_ready, j + 1)
                    pe.wait_ge(p_low_ready, j + 1)
                    pe.wait_ge(lora_low_ready, 1)
                    if j == 1:
                        pe.wait_ge(lora_spread, 1)
                if j == 0 and n == 1:
                    pe.wait_ge(p_low_ready, NP2)
                if NY * j + n >= 2:
                    pe.wait_ge(y_added, NY * j + n - 1)
                for o in (2 * n, 2 * n + 1):
                    for part in range(2):
                        mm = nc.tensor.matmul(y_ps[:, n % 2, BANK * (o % 2):BANK * (o % 2 + 1)],
                                              p_map[:, j, P * o:P * (o + 1)], v[:, j % 2, part],
                                              start=(part == 0), stop=(part == 1))
                mm.then_inc(y_done, 1)

            for c in range(WCH):
                multiply_w(c)
                if c == 0:
                    spread_g()
            multiply_b(0, 0)
            multiply_b(0, 1)
            make_uzd(0)
            count_votes(0)
            multiply_b(1, 0)
            multiply_b(1, 1)
            for j in range(NP2):
                if j + 1 < NP2:
                    make_uzd(j + 1)
                make_y(j, 0)
                if j + 1 < NP2:
                    count_votes(j + 1)
                make_y(j, 1)
                if j + 2 < NP2:
                    multiply_b(j + 2, 0)
                make_y(j, 2)
                if j + 2 < NP2:
                    multiply_b(j + 2, 1)
                make_y(j, 3)


def kernel(x, itok_B_3_7, L0_cond_A, L0_cond_B, L0_ffn_W_up, L0_ffn_gate_w, L0_ffn_expert_bias,
           L0_ffn_lora_A, L0_ffn_lora_B):
    import numpy as np
    import concourse.bacc as bacc
    from concourse.bass_utils import run_bass_kernel_spmd

    x, ids = np.asarray(x), np.asarray(itok_B_3_7)
    A, B, W = np.asarray(L0_cond_A), np.asarray(L0_cond_B), np.asarray(L0_ffn_W_up)
    gate, bias = np.asarray(L0_ffn_gate_w), np.asarray(L0_ffn_expert_bias)
    lora_a, lora_b = np.asarray(L0_ffn_lora_A), np.asarray(L0_ffn_lora_B)
    NB, T, H = x.shape
    NA, _, R = A.shape
    E, RL, _ = lora_a.shape
    KB, WCH = H // P, 4

    first = [e for e in range(E) for f in range(e + 1, E)]
    second = [f for e in range(E) for f in range(e + 1, E)]
    votes = np.zeros((len(first), P), np.float32)
    needed = np.zeros((P, 1), np.float32)
    for side in (Q, 3 * Q):
        for e in range(E):
            cols = slice(side + RL * e, side + RL * (e + 1))
            needed[cols] = E - 1 - e
            for n, (a, b) in enumerate(zip(first, second)):
                votes[n, cols] = (a == e) * 1.0 - (b == e) * 1.0
    arrays = {
        "x": x.reshape(NB // 2, 2, T, 2, KB // 2, P).transpose(0, 3, 5, 4, 1, 2)
        .reshape(NB // 2, 2, P, KB // 2, 2 * T),
        "ids": ids.reshape(1, NB),
        "cond_a": A.reshape(NA, KB, P, R).transpose(2, 0, 1, 3).reshape(P, NA, KB * R),
        "cond_b": B.reshape(NA, R, KB, P).transpose(3, 0, 2, 1).reshape(P, NA, KB * R),
        "w_up": W.reshape(H, WCH, KB // WCH, P).transpose(1, 3, 2, 0),
        "lora_a_gate": np.concatenate([lora_a.reshape(E * RL, H), gate]).reshape(E * RL + E, KB, P)
        .transpose(2, 1, 0),
        "lora_b": lora_b.transpose(0, 2, 1).reshape(E * RL, H),
        "bias_pairs": np.stack([bias[first], bias[second]], axis=1),
        "pair_votes": votes,
        "votes_needed": needed,
    }
    nc = bacc.Bacc("TRN2", target_bir_lowering=False, num_devices=1)
    arrays = {f"in_{name}": np.ascontiguousarray(a) for name, a in arrays.items()}
    ins = [nc.dram_tensor(name, a.shape, mybir.dt.from_np(a.dtype), kind="ExternalInput").ap()
           for name, a in arrays.items()]
    y = nc.dram_tensor("out_y", (NB // 2, KB // 2, P, 2, 2 * T), F32, kind="ExternalOutput").ap()
    adaln_ffn(nc, *ins, y)
    r = run_bass_kernel_spmd(nc, [arrays], core_ids=[0])
    y = r.results[0]["out_y"].reshape(NB // 2, KB // 2, P, 2, 2, T).transpose(0, 4, 5, 1, 3, 2)
    return np.ascontiguousarray(y).reshape(NB, T, H)
```
